# Optimizing a Trainium2 kernel written in Bass

```python
import numpy as np
import jax
import jax.numpy as jnp

def _softmax(x, axis=-1):
    return jax.nn.softmax(x, axis=axis)

def _gelu(x):
    return jax.nn.gelu(x, approximate=True)

def _silu(x):
    return jax.nn.silu(x)

def _sigmoid(x):
    return jax.nn.sigmoid(x)

def _layernorm(x, axis=-1, eps=1e-05):
    m = jnp.mean(x, axis=axis, keepdims=True)
    v = jnp.var(x, axis=axis, keepdims=True)
    return (x - m) / jnp.sqrt(v + eps)

def _scatter_add(tgt, idx, src, axis=0):
    return tgt.at[idx].add(src)

def _segment_sum(src, seg, n):
    return jax.ops.segment_sum(src, seg, n)
kernel_name = 'mk_adaln_ffn_d1_seqx_r2_a88f7d'

def setup_inputs(seed: int=0):
    np.random.seed(seed)
    _w = jnp.asarray

    def _rec_inputs():
        import jax
        import jax.numpy as jnp
        _rk = jax.random.key(seed)
        x = -0.000125 + 0.9999 * jax.random.normal(jax.random.fold_in(_rk, 1), (32, 128, 2048), jnp.float32)
        _lenS = 128 - jax.random.randint(jax.random.fold_in(_rk, 7), (32,), 0, max(1, 128 // 4) + 1, jnp.int32)
        _lenS2 = 128 - jax.random.randint(jax.random.fold_in(_rk, 8), (32,), 0, max(1, 128 // 4) + 1, jnp.int32)
        cond_128 = 0.0061147 + 1.02565 * jax.random.normal(jax.random.fold_in(_rk, 11), (32, 128), jnp.float32)
        return (x, cond_128)
    x, cond_128 = _rec_inputs()

    def _L0_cond_setup():
        import jax, jax.numpy as jnp
        import numpy as np
        K = 8
        T = 1.0
        D_EMBD = 128
        IN_C = 128
        OUT_C = 128
        BS = 32
        H = 2048
        HID = 128
        key = jax.random.key(seed)
        ks = jax.random.split(key, 10)
        s = lambda fan_in: 1.0 / np.sqrt(fan_in)
        return {'x': jax.random.normal(ks[0], (BS, IN_C, H), dtype=jnp.float32), 'embedding': jax.random.normal(ks[1], (BS, D_EMBD), dtype=jnp.float32), 'W0': jax.random.normal(ks[2], (D_EMBD, HID), dtype=jnp.float32) * s(D_EMBD), 'b0': jnp.zeros((HID,), dtype=jnp.float32), 'W1': jax.random.normal(ks[3], (HID, HID), dtype=jnp.float32) * s(HID), 'b1': jnp.zeros((HID,), dtype=jnp.float32), 'W2': jax.random.normal(ks[4], (HID, K), dtype=jnp.float32) * s(HID), 'b2': jnp.zeros((K,), dtype=jnp.float32), 'weight': jax.random.normal(ks[5], (K, OUT_C, IN_C, 1), dtype=jnp.float32) * s(IN_C), 'bias_k': jax.random.normal(ks[6], (K, OUT_C), dtype=jnp.float32) * 0.1}
    _L0_cond_all = _L0_cond_setup()
    _L0_cond_in = {k: v for k, v in _L0_cond_all.items() if k in ('W0', 'b0', 'W1', 'b1', 'W2', 'b2', 'weight', 'bias_k')}
    del _L0_cond_all

    def _L0_ffn_setup():
        import jax, jax.numpy as jnp
        import numpy as np
        IN_F = 2048
        OUT_F = 2048
        N_CLUSTERS = 64
        THRESHOLD = 0.01
        TEMPERATURE = 0.1
        BATCH, SEQ = (4, 1024)
        key = jax.random.key(seed)
        k1, k2, k3, k4, k5 = jax.random.split(key, 5)
        s = 1.0 / np.sqrt(IN_F)
        return {'input': jax.random.normal(k1, (BATCH, SEQ, IN_F), dtype=jnp.float32), 'weight': jax.random.normal(k2, (OUT_F, IN_F), dtype=jnp.float32) * s, 'bias': jax.random.uniform(k3, (OUT_F,), dtype=jnp.float32, minval=-s, maxval=s), 'centroids': jax.random.normal(k4, (N_CLUSTERS, IN_F), dtype=jnp.float32) * s, 'assignments': jax.random.randint(k5, (OUT_F,), 0, N_CLUSTERS, dtype=jnp.int32)}
    _L0_ffn_all = _L0_ffn_setup()
    _L0_ffn_in = {k: v for k, v in _L0_ffn_all.items() if k in ('weight', 'bias', 'centroids', 'assignments')}
    del _L0_ffn_all
    return {'x': x, 'cond_128': cond_128, 'L0_cond_W0': _L0_cond_in['W0'], 'L0_cond_b0': _L0_cond_in['b0'], 'L0_cond_W1': _L0_cond_in['W1'], 'L0_cond_b1': _L0_cond_in['b1'], 'L0_cond_W2': _L0_cond_in['W2'], 'L0_cond_b2': _L0_cond_in['b2'], 'L0_cond_weight': _L0_cond_in['weight'], 'L0_cond_bias_k': _L0_cond_in['bias_k'], 'L0_ffn_weight': _L0_ffn_in['weight'], 'L0_ffn_bias': _L0_ffn_in['bias'], 'L0_ffn_centroids': _L0_ffn_in['centroids'], 'L0_ffn_assignments': _L0_ffn_in['assignments']}

def reference(x, cond_128, L0_cond_W0, L0_cond_b0, L0_cond_W1, L0_cond_b1, L0_cond_W2, L0_cond_b2, L0_cond_weight, L0_cond_bias_k, L0_ffn_weight, L0_ffn_bias, L0_ffn_centroids, L0_ffn_assignments):
    import jax
    import jax.numpy as jnp

    def _L0_cond_ref(x, embedding, W0, b0, W1, b1, W2, b2, weight, bias_k):
        import jax, jax.numpy as jnp
        import numpy as np
        K = 8
        T = 1.0
        D_EMBD = 128
        IN_C = 128
        OUT_C = 128
        BS = 32
        H = 2048
        HID = 128
        h = jax.nn.gelu(embedding @ W0 + b0, approximate=False)
        h = jax.nn.gelu(h @ W1 + b1, approximate=False)
        att = jax.nn.softmax((h @ W2 + b2) / T, axis=-1)
        agg_w = jnp.einsum('bk,koi->boi', att, weight[..., 0])
        agg_b = att @ bias_k
        out = jnp.einsum('boi,bih->boh', agg_w, x) + agg_b[:, :, None]
        return out

    def _L0_ffn_ref(input, weight, bias, centroids, assignments):
        import jax, jax.numpy as jnp
        import numpy as np
        IN_F = 2048
        OUT_F = 2048
        N_CLUSTERS = 64
        THRESHOLD = 0.01
        TEMPERATURE = 0.1
        BATCH, SEQ = (4, 1024)
        shape = input.shape
        x = input.reshape(-1, shape[-1])
        dots = jax.nn.softmax(x @ centroids.T / TEMPERATURE, axis=-1)
        hits = dots > THRESHOLD
        query_sel = jnp.any(hits, axis=1)
        cluster_sel = jnp.any(hits, axis=0)
        row_sel = cluster_sel[assignments]
        dense = x @ weight.T + bias
        out = jnp.where(query_sel[:, None] & row_sel[None, :], dense, jnp.zeros((), dense.dtype))
        return out.reshape(*shape[:-1], -1)
    x = x + _L0_ffn_ref(_L0_cond_ref(x, cond_128, L0_cond_W0, L0_cond_b0, L0_cond_W1, L0_cond_b1, L0_cond_W2, L0_cond_b2, L0_cond_weight, L0_cond_bias_k), L0_ffn_weight, L0_ffn_bias, L0_ffn_centroids, L0_ffn_assignments)
    return x

_drawn_inputs = setup_inputs


def setup_inputs(seed=0):
    import zlib

    import numpy as np

    out = dict(_drawn_inputs(seed))
    spreads = {'L0_cond_b0': (0.0, 0.516), 'L0_cond_b1': (0.0, 0.322), 'L0_cond_b2': (0.0, 0.292)}
    factors = {'L0_ffn_bias': 4.744}
    for name, (base, spread) in spreads.items():
        noise = np.random.default_rng([zlib.crc32(name.encode()), seed]).standard_normal(out[name].shape)
        drawn = base * np.exp(spread * noise) if base else spread * noise
        out[name] = jnp.asarray(drawn.astype(out[name].dtype))
    for name, factor in factors.items():
        out[name] = (out[name] * factor).astype(out[name].dtype)
    return out
```

```python
from contextlib import ExitStack

import numpy as np

import concourse.bass as bass
from concourse import mybir

ALU = mybir.AluOpType
ACT = mybir.ActivationFunctionType
F32 = mybir.dt.float32
F32R = mybir.dt.float32r
BF16 = mybir.dt.bfloat16
I32 = mybir.dt.int32
U8 = mybir.dt.uint8
AX_X = mybir.AxisListType.X

P = 128
BANK = 512
GROUP = 4
THRESHOLD = 0.01
INV_TEMPERATURE = 10.0



def adaln_ffn_kernel(nc, x, xT, w_first, w_second, cond_T, W0, b0, W1, b1, W2, b2, wk_T, bias_k_T,
                     ffn_bias, assignments, out):
    B, _, H = x.shape
    KT = H // P
    HALF = H // 2
    NC = w_first.shape[2] - HALF
    WIDE = HALF + NC
    NG = KT // GROUP
    K = W2.shape[1]
    HID = W0.shape[1]
    WSLOTS = 4

    CHUNKS = [[(0, 384), (384, 768), (768, WIDE)], [(0, BANK), (BANK, HALF)]]
    DOTS_AT = CHUNKS[0][2][1] - CHUNKS[0][2][0]
    assert DOTS_AT + NC <= BANK and KT % GROUP == 0 and B % 2 == 0

    with ExitStack() as ctx:
        def sb(name, shape, dt):
            return ctx.enter_context(nc.sbuf_tensor(name, shape, dt))

        def sem(name):
            return ctx.enter_context(nc.semaphore(name))

        w_hi = sb("w_hi", [P, KT, WIDE], F32R)
        w_lo = sb("w_lo", [P, KT, WIDE], F32R)
        x_hi = sb("x_hi", [P, KT, P], F32R)
        x_lo = sb("x_lo", [P, KT, P], F32R)
        x_raw = sb("x_raw", [P, KT, P], F32)
        stage = sb("stage", [P, WSLOTS * WIDE], F32)
        z_hi = sb("z_hi", [P, WIDE], F32R)
        z_lo = sb("z_lo", [P, WIDE], F32R)
        w_sum = sb("w_sum", [P, WIDE], F32)
        rowsum = sb("rowsum", [P, WIDE], F32)
        bias_bc = sb("bias_bc", [P, HALF], F32)
        row_mask = sb("row_mask", [P, H], U8)
        temp = sb("temp", [P, HALF], F32)
        first_half = sb("first_half", [P, 2, HALF], F32)
        wk = sb("wk", [P, P, K], F32)
        onehot = sb("onehot", [P, HALF], BF16)
        att_bc = sb("att_bc", [P, B * K], F32)
        agg_b = sb("agg_b", [P, B], F32)
        agg_w = sb("agg_w", [P, P], F32)
        agg_hi = sb("agg_hi", [P, P], F32R)
        agg_lo = sb("agg_lo", [P, P], F32R)
        bkT = sb("bkT", [P, K], F32)
        scores = sb("scores", [P, NC], F32)
        probs = sb("probs", [P, NC], F32)
        any_hit = sb("any_hit", [P, 2, NC], F32)
        sel_bc = sb("sel_bc", [P, P], BF16)
        query_sel = sb("query_sel", [P, B], F32)
        row_max = sb("row_max", [P, 1], F32)
        neg_max = sb("neg_max", [P, 1], F32)
        exp_sum = sb("exp_sum", [P, 1], F32)
        exp_inv = sb("exp_inv", [P, 1], F32)
        ones = sb("ones", [P, P], F32)
        cluster_id = sb("cluster_id", [P, 1], F32)

        early = first_half[:, :, :].rearrange("p a n -> p (a n)")
        w0_sb = early[:, 0:128]
        w1_sb = early[:, 128:256]
        cond_sb = early[:, 256:288]
        h1 = early[:, 288:320]
        h2 = early[:, 320:352]
        w2_sb = early[:, 352:360]
        b0_sb = early[:, 360:361]
        b1_sb = early[:, 361:362]
        b2_sb = early[0:1, 364:372]
        att_max = early[0:B, 372:373]
        att_neg = early[0:B, 373:374]
        att_sum = early[0:B, 374:375]
        att_inv = early[0:B, 375:376]
        att_exp = early[0:B, 376:384]
        att = early[0:B, 384:392]
        ident = early[0:B, 400:432]
        att_diag = early[0:B, 512:512 + B * K]
        assign_bc = temp[:, :].bitcast(I32)

        z_ps = [ctx.enter_context(nc.psum_tensor(f"z_ps{i}", [P, 3, BANK], F32)) for i in range(2)]
        d_ps = ctx.enter_context(nc.psum_tensor("d_ps", [P, 2, BANK], F32))
        h1_ps, h2_ps = d_ps[:, 0, 0:32], d_ps[:, 0, 32:64]
        logit_ps = d_ps[0:B, 0, 64:64 + K]
        att_ps = d_ps[:, 1, 0:B * K]

        dram_half = nc.dram_tensor("dense_first_half", [B, P, HALF], F32, kind="Internal").ap()

        x_start_in = sem("x_start_in")
        x_raw_in = sem("x_raw_in")
        w_raw_in = [sem(f"w_raw_in{i}") for i in range(WSLOTS)]
        cond_in = sem("cond_in")
        bias_in = sem("bias_in")
        const_in = sem("const_in")
        assign_in = sem("assign_in")
        half_out = [sem(f"half_out{i}") for i in range(2)]
        rest_in = [sem(f"rest_in{i}") for i in range(2)]
        out_done = [sem(f"out_done{i}") for i in range(2)]
        ones_ready = sem("ones_ready")
        zero_ready = sem("zero_ready")
        ident_ready = sem("ident_ready")
        cluster_id_ready = sem("cluster_id_ready")
        onehot_ready = sem("onehot_ready")
        any_hit_zeroed = sem("any_hit_zeroed")
        w_hi_ready = sem("w_hi_ready")
        w_lo_ready = sem("w_lo_ready")
        w_summed = sem("w_summed")
        x_hi_ready = sem("x_hi_ready")
        x_lo_ready = sem("x_lo_ready")
        z_hi_ready = sem("z_hi_ready")
        z_lo_ready = sem("z_lo_ready")
        tiles_used = sem("tiles_used")
        dots_ready = sem("dots_ready")
        dense_ready = sem("dense_ready")
        dense_drained = sem("dense_drained")
        rowsum_made = sem("rowsum_made")
        cluster_sum_ready = sem("cluster_sum_ready")
        rowsum_ready = sem("rowsum_ready")
        h1_made = sem("h1_made")
        h1_ready = sem("h1_ready")
        h2_made = sem("h2_made")
        h2_ready = sem("h2_ready")
        logits_made = sem("logits_made")
        att_max_ready = sem("att_max_ready")
        att_neg_ready = sem("att_neg_ready")
        att_exp_ready = sem("att_exp_ready")
        att_inv_ready = sem("att_inv_ready")
        att_ready = sem("att_ready")
        att_diag_ready = sem("att_diag_ready")
        att_spread = sem("att_spread")
        att_bc_ready = sem("att_bc_ready")
        agg_b_terms = sem("agg_b_terms")
        agg_b_ready = sem("agg_b_ready")
        agg_terms = sem("agg_terms")
        agg_summed = sem("agg_summed")
        agg_hi_ready = sem("agg_hi_ready")
        agg_ready = sem("agg_ready")
        scores_ready = sem("scores_ready")
        row_max_ready = sem("row_max_ready")
        neg_max_ready = sem("neg_max_ready")
        probs_ready = sem("probs_ready")
        exp_inv_ready = sem("exp_inv_ready")
        hit_ready = sem("hit_ready")
        hits_merged = sem("hits_merged")
        any_hit_doubled = sem("any_hit_doubled")
        counts_made = sem("counts_made")
        sel_ready = sem("sel_ready")
        mask_made = sem("mask_made")
        mask_ready = sem("mask_ready")
        offset_ready = sem("offset_ready")
        half_ready = sem("half_ready")
        masked_ready = sem("masked_ready")
        half_masked = sem("half_masked")
        out_ready = sem("out_ready")

        def slot(t, width):
            return stage[:, (t % WSLOTS) * WIDE:(t % WSLOTS) * WIDE + width]

        def rest(par):
            return stage[:, par * H:(par + 1) * H]

        def width_of(t):
            return WIDE if t < KT else HALF

        def xg(t, g):
            return t[:, g * GROUP:(g + 1) * GROUP, :]

        def turn(b, par):
            return 8 * b + (8 if par else 16)

        block = ctx.enter_context(nc.Block())

        @block.sync
        def _(sp):
            def load_x(b, s):
                sp.wait_ge(x_lo_ready, NG * s)
                sp.dma_start(x_raw[:, :, :], xT[b, :, :, :]).then_inc(x_raw_in, 16)

            def load_w(t):
                if t >= WSLOTS:
                    sp.wait_ge(w_lo_ready, t - WSLOTS + 1)
                    sp.wait_ge(w_summed, t - WSLOTS + 1)
                src = w_first[t, :, :] if t < KT else w_second[t - KT, :, :]
                sp.dma_start(slot(t, width_of(t)), src).then_inc(w_raw_in[t % WSLOTS], 16)

            def store_half(b, par):
                sp.wait_ge(half_ready, b + 1)
                sp.dma_start(dram_half[b, :, :], first_half[:, par, :]).then_inc(half_out[par], 16)

            def load_rest(b, par):
                sp.dma_start(rest(par), x[b, :, :]).then_inc(rest_in[par], 16)
                sp.dma_start(first_half[:, par, :], dram_half[b, :, :]).then_inc(rest_in[par], 16)

            def store_out(b, par):
                sp.wait_ge(out_ready, b + 1)
                sp.dma_start(out[b, :, :], rest(par)).then_inc(out_done[par], 16)

            sp.dma_start(x_raw[:, 0:GROUP, :], xT[0, :, 0:GROUP, :]).then_inc(x_start_in, 16)
            load_w(0)
            sp.dma_start(x_raw[:, GROUP:KT, :], xT[0, :, GROUP:KT, :]).then_inc(x_raw_in, 16)
            for t in range(1, KT):
                load_w(t)
                if t == WSLOTS * 3:
                    sp.dma_start(bias_bc[:, :], ffn_bias[0:HALF].partition_broadcast(P)).then_inc(bias_in, 16)
            load_x(1, 1)

            def step_first(b, par):
                load_x(b + 1, b + 1)
                store_half(b - 1, 1 - par)

            step_first(1, 1)
            step_first(2, 0)
            with sp.Fori(0, B // 2 - 2) as pair:
                b = 2 * pair + 3
                step_first(b, 1)
                step_first(b + 1, 0)
            load_x(0, B)
            for t in range(KT, KT + 2 * GROUP):
                load_w(t)
            store_half(B - 2, 0)
            for t in range(KT + 2 * GROUP, 2 * KT):
                load_w(t)
            load_x(1, B + 1)
            store_half(B - 1, 1)
            sp.wait_ge(offset_ready, B)
            sp.dma_start(bias_bc[:, :], ffn_bias[HALF:H].partition_broadcast(P)).then_inc(bias_in, 16)
            sp.wait_ge(w_lo_ready, 2 * KT)
            sp.wait_ge(w_summed, 2 * KT)
            for par in range(2):
                sp.wait_ge(half_out[par], turn(B - 2 + par, par))
            load_rest(0, 0)
            load_rest(1, 1)

            def step_second(b, par, last):
                if not last:
                    load_x(b + 1, B + b + 1)
                store_out(b - 1, 1 - par)
                if not last:
                    sp.wait_ge(out_done[1 - par], turn(b - 1, 1 - par))
                    load_rest(b + 1, 1 - par)

            step_second(1, 1, False)
            step_second(2, 0, False)
            with sp.Fori(0, B // 2 - 2) as pair:
                b = 2 * pair + 3
                step_second(b, 1, False)
                step_second(b + 1, 0, False)
            step_second(B - 1, 1, True)
            store_out(B - 1, 1)
            for par in range(2):
                sp.wait_ge(out_done[par], turn(B - 2 + par, par))

        @block.gpsimd
        def _(pool):
            nc.gpsimd.memset(ones[:, :], 1.0).then_inc(ones_ready, 1)
            nc.gpsimd.memset(ident, 0.0).then_inc(zero_ready, 1)
            pool.wait_ge(zero_ready, 1)
            nc.gpsimd.affine_select(out=ident, in_=ident, compare_op=ALU.not_equal, fill=1.0, base=0,
                                    pattern=[[-1, B]], channel_multiplier=1).then_inc(ident_ready, 1)
            for g in range(2):
                pool.wait_ge(ident_ready, 1)
                if g:
                    pool.wait_ge(cluster_id_ready, g)
                nc.gpsimd.iota(cluster_id[g * NC:(g + 1) * NC, :], [[0, 1]], base=0, channel_multiplier=1,
                               allow_small_or_imprecise_dtypes=True).then_inc(cluster_id_ready, 1)
            pool.wait_ge(ones_ready, 1)
            pool.wait_ge(cluster_id_ready, 2)
            for t in range(2 * KT):
                width = width_of(t)
                pool.wait_ge(w_raw_in[t % WSLOTS], 16 * (t // WSLOTS + 1))
                if t == KT:
                    pool.wait_ge(rowsum_made, 1)
                if t % KT == 0:
                    nc.gpsimd.tensor_copy(w_sum[:, 0:width], slot(t, width)).then_inc(w_summed, 1)
                else:
                    pool.wait_ge(w_summed, t)
                    nc.gpsimd.tensor_tensor(w_sum[:, 0:width], w_sum[:, 0:width], slot(t, width),
                                            ALU.add).then_inc(w_summed, 1)

        @block.scalar
        def _(act):
            def split_w(t):
                width = width_of(t)
                act.wait_ge(w_raw_in[t % WSLOTS], 16 * (t // WSLOTS + 1))
                if t >= KT and t % GROUP == 0:
                    act.wait_ge(tiles_used, NG * (B - 1) + (t - KT) // GROUP + 1)
                nc.scalar.copy(w_hi[:, t % KT, 0:width], slot(t, width)).then_inc(w_hi_ready, 1)

            def split_x(s, g):
                act.wait_ge(x_raw_in, 16 * (s + 1))
                act.wait_ge(tiles_used, NG * s - NG + g + 1)
                nc.scalar.copy(xg(x_hi, g), xg(x_raw, g)).then_inc(x_hi_ready, 1)

            def split_z(s, par, phase, wait_before=True):
                act.wait_ge(tiles_used, NG * s + NG)
                if wait_before:
                    act.wait_ge(dense_ready, s)
                if phase == 0:
                    nc.scalar.copy(z_hi[:, 0:768].rearrange("p (a n) -> p a n", a=2), z_ps[par][:, 0:2, 0:384])
                    nc.scalar.copy(z_hi[:, 768:WIDE], z_ps[par][:, 2, 0:WIDE - 768]).then_inc(z_hi_ready, 1)
                else:
                    nc.scalar.copy(z_hi[:, 0:HALF].rearrange("p (a n) -> p a n", a=2),
                                   z_ps[par][:, 0:2, :]).then_inc(z_hi_ready, 1)

            def exp_scores(s):
                act.wait_ge(neg_max_ready, s + 1)
                nc.scalar.activation(probs[:, :], scores[:, :], ACT.Exp, bias=neg_max[:, :],
                                     scale=INV_TEMPERATURE, accum_out=exp_sum[:, :]).then_inc(probs_ready, 1)

            act.dma_start(cond_sb, cond_T).then_inc(cond_in, 16)
            act.dma_start(w0_sb, W0).then_inc(cond_in, 16)
            act.dma_start(b0_sb, b0.rearrange("(p a) -> p a", a=1)).then_inc(cond_in, 16)
            act.dma_start(w1_sb, W1).then_inc(cond_in, 16)
            act.dma_start(b1_sb, b1.rearrange("(p a) -> p a", a=1)).then_inc(cond_in, 16)
            act.dma_start(w2_sb, W2).then_inc(cond_in, 16)
            act.dma_start(b2_sb, b2.rearrange("(a k) -> a k", a=1)).then_inc(cond_in, 16)
            for g in range(2):
                act.dma_start(assign_bc[g * NC:(g + 1) * NC, :],
                              assignments[g * HALF:(g + 1) * HALF].partition_broadcast(NC)).then_inc(assign_in, 16)
            act.dma_start(wk[:, :, :], wk_T).then_inc(const_in, 16)
            act.dma_start(bkT[:, :], bias_k_T).then_inc(const_in, 16)

            for t in range(KT):
                if t % GROUP == 0:
                    act.wait_ge(x_start_in if t == 0 else x_raw_in, 16)
                    nc.scalar.copy(xg(x_hi, t // GROUP), xg(x_raw, t // GROUP)).then_inc(x_hi_ready, 1)
                split_w(t)
                if t == 2:
                    act.wait_ge(h1_made, 1)
                    act.wait_ge(cond_in, 16 * 7)
                    nc.scalar.activation(h1, h1_ps, ACT.Gelu, bias=b0_sb).then_inc(h1_ready, 1)
                if t == 4:
                    act.wait_ge(h2_made, 1)
                    nc.scalar.activation(h2, h2_ps, ACT.Gelu, bias=b1_sb).then_inc(h2_ready, 1)
                if t == 8:
                    act.wait_ge(att_neg_ready, 1)
                    nc.scalar.activation(att_exp, logit_ps, ACT.Exp, bias=att_neg,
                                         accum_out=att_sum).then_inc(att_exp_ready, 1)
            for g in range(NG - 1):
                split_x(1, g)

            def step(b, s, par, phase, last=False):
                split_z(s - 1, 1 - par, phase)
                split_x(s, NG - 1)
                if not last:
                    split_x(s + 1, 0)
                if phase == 0:
                    exp_scores(s - 1)
                for g in range(1, NG - 1):
                    if not last:
                        split_x(s + 1, g)

            step(1, 1, 1, 0)
            step(2, 2, 0, 0)
            with act.Fori(0, B // 2 - 2) as pair:
                b = 2 * pair + 3
                step(b, b, 1, 0)
                step(b + 1, b + 1, 0, 0)
            split_z(B - 2, 0, 0)
            split_x(B - 1, NG - 1)
            for g in range(NG - 1):
                split_x(B, g)
                for t in range(KT + g * GROUP, KT + (g + 1) * GROUP):
                    split_w(t)
                if g == 0:
                    exp_scores(B - 2)
            split_z(B - 1, 1, 0)
            split_x(B, NG - 1)
            for t in range(2 * KT - GROUP, 2 * KT):
                split_w(t)
            split_x(B + 1, 0)
            exp_scores(B - 1)
            for g in range(1, NG - 1):
                split_x(B + 1, g)
            step(1, B + 1, 1, 1)
            step(2, B + 2, 0, 1)
            with act.Fori(0, B // 2 - 2) as pair:
                b = 2 * pair + 3
                step(b, b + B, 1, 1)
                step(b + 1, b + (B + 1), 0, 1)
            step(B - 1, 2 * B - 1, 1, 1, last=True)
            split_z(2 * B - 1, 1, 1)

        @block.vector
        def _(dve):
            def split_w(t):
                width = width_of(t)
                dve.wait_ge(w_hi_ready, t + 1)
                nc.vector.tensor_tensor(w_lo[:, t % KT, 0:width], slot(t, width),
                                        w_hi[:, t % KT, 0:width].bitcast(F32), ALU.subtract).then_inc(w_lo_ready, 1)

            def split_x(s, g):
                dve.wait_ge(x_hi_ready, NG * s + g + 1)
                nc.vector.tensor_tensor(xg(x_lo, g), xg(x_raw, g), xg(x_hi, g).bitcast(F32),
                                        ALU.subtract).then_inc(x_lo_ready, 1)

            def split_z(s, par, phase):
                dve.wait_ge(z_hi_ready, s + 1)
                if phase == 0:
                    nc.vector.tensor_tensor(z_lo[:, 0:768].rearrange("p (a n) -> p a n", a=2),
                                            z_ps[par][:, 0:2, 0:384],
                                            z_hi[:, 0:768].bitcast(F32).rearrange("p (a n) -> p a n", a=2),
                                            ALU.subtract)
                    nc.vector.tensor_tensor(z_lo[:, 768:WIDE], z_ps[par][:, 2, 0:WIDE - 768],
                                            z_hi[:, 768:WIDE].bitcast(F32), ALU.subtract).then_inc(z_lo_ready, 1)
                else:
                    nc.vector.tensor_tensor(z_lo[:, 0:HALF].rearrange("p (a n) -> p a n", a=2),
                                            z_ps[par][:, 0:2, :],
                                            z_hi[:, 0:HALF].bitcast(F32).rearrange("p (a n) -> p a n", a=2),
                                            ALU.subtract).then_inc(z_lo_ready, 1)

            def mix_weights(b, s, first=False, outs=None):
                if outs is not None:
                    dve.wait_ge(out_ready, outs)
                if not first:
                    dve.wait_ge(dense_ready, s)
                att_b = att_bc[:, bass.ds(b * K, K)].unsqueeze(1).broadcast_to([P, P, K])
                nc.vector.tensor_tensor(temp[:, :].rearrange("p (o k) -> p o k", k=K), wk[:, :, :], att_b,
                                        ALU.mult).then_inc(agg_terms, 1)
                dve.wait_ge(agg_terms, s + 1)
                nc.vector.tensor_reduce(agg_w[:, :], temp[:, :].rearrange("p (o k) -> p o k", k=K), AX_X,
                                        ALU.add).then_inc(agg_summed, 1)
                dve.wait_ge(agg_summed, s + 1)
                nc.vector.tensor_copy(agg_hi[:, :], agg_w[:, :]).then_inc(agg_hi_ready, 1)
                dve.wait_ge(agg_hi_ready, s + 1)
                nc.vector.tensor_tensor(agg_lo[:, :], agg_w[:, :], agg_hi[:, :].bitcast(F32),
                                        ALU.subtract).then_inc(agg_ready, 1)

            def start_softmax(b, par):
                dve.wait_ge(dots_ready, b + 1)
                nc.vector.scalar_tensor_tensor(out=scores[:, :], in0=rowsum[:, HALF:WIDE],
                                               scalar=agg_b[:, bass.ds(b, 1)],
                                               in1=z_ps[par][:, 2, DOTS_AT:DOTS_AT + NC],
                                               op0=ALU.mult, op1=ALU.add).then_inc(scores_ready, 1)
                dve.wait_ge(scores_ready, b + 1)
                nc.vector.tensor_reduce(row_max[:, :], scores[:, :], AX_X, ALU.max).then_inc(row_max_ready, 1)
                dve.wait_ge(row_max_ready, b + 1)
                nc.vector.tensor_scalar(neg_max[:, :], row_max[:, :], -INV_TEMPERATURE, None,
                                        ALU.mult).then_inc(neg_max_ready, 1)

            def find_hits(b):
                dve.wait_ge(probs_ready, b + 1)
                nc.vector.reciprocal(exp_inv[:, :], exp_sum[:, :]).then_inc(exp_inv_ready, 1)
                dve.wait_ge(exp_inv_ready, b + 1)
                nc.vector.tensor_scalar(probs[:, :], probs[:, :], exp_inv[:, 0:1], THRESHOLD,
                                        ALU.mult, ALU.is_gt).then_inc(hit_ready, 1)
                dve.wait_ge(hit_ready, b + 1)
                nc.vector.tensor_reduce(query_sel[:, bass.ds(b, 1)], probs[:, :], AX_X, ALU.max)
                nc.vector.tensor_tensor(any_hit[:, 0, :], any_hit[:, 0, :], probs[:, :],
                                        ALU.max).then_inc(hits_merged, 1)

            def make_offset(dst, b, s):
                nc.vector.scalar_tensor_tensor(out=dst, in0=rowsum[:, 0:HALF], scalar=agg_b[:, bass.ds(b, 1)],
                                               in1=bias_bc[:, :], op0=ALU.mult, op1=ALU.add).then_inc(offset_ready, 1)
                dve.wait_ge(offset_ready, s + 1)

            def dense_of(dst, s, ready):
                dve.wait_ge(dense_ready, s + 1)
                nc.vector.tensor_tensor(dst, dst, d_ps[:, :, :].rearrange("p a n -> p (a n)"),
                                        ALU.add).then_inc(ready, 1)

            def finish_first(b, par):
                if not isinstance(b, int) or b >= 2:
                    dve.wait_ge(half_out[par], turn(b, par) - 16)
                make_offset(first_half[:, par, :], b, b)
                dense_of(first_half[:, par, :], b, half_ready)

            def finish_second(b, s, par):
                rows = rest(par)
                make_offset(temp[:, :], b, s)
                dense_of(temp[:, :], s, dense_drained)
                dve.wait_ge(dense_drained, b + 1)
                nc.vector.scalar_tensor_tensor(out=temp[:, :], in0=temp[:, :], scalar=query_sel[:, bass.ds(b, 1)],
                                               in1=row_mask[:, HALF:H], op0=ALU.mult,
                                               op1=ALU.mult).then_inc(masked_ready, 1)
                dve.wait_ge(rest_in[par], 2 * turn(b, par))
                nc.vector.scalar_tensor_tensor(out=first_half[:, par, :], in0=first_half[:, par, :],
                                               scalar=query_sel[:, bass.ds(b, 1)], in1=row_mask[:, 0:HALF],
                                               op0=ALU.mult, op1=ALU.mult).then_inc(half_masked, 1)
                dve.wait_ge(half_masked, b + 1)
                nc.vector.tensor_tensor(rows[:, 0:HALF], rows[:, 0:HALF], first_half[:, par, :], ALU.add)
                dve.wait_ge(masked_ready, b + 1)
                nc.vector.tensor_tensor(rows[:, HALF:H], rows[:, HALF:H], temp[:, :], ALU.add).then_inc(out_ready, 1)

            def copy_rowsum(phase):
                dve.wait_ge(rowsum_made, phase + 1)
                if phase == 0:
                    nc.vector.tensor_copy(rowsum[:, HALF:WIDE], z_ps[1][:, 2, 0:NC]).then_inc(cluster_sum_ready, 1)
                nc.vector.tensor_copy(rowsum[:, 0:HALF],
                                      d_ps[:, :, :].rearrange("p a n -> p (a n)")).then_inc(rowsum_ready, 1)

            nc.vector.memset(any_hit[:, :, :], 0.0).then_inc(any_hit_zeroed, 1)
            for t in range(KT):
                if t % GROUP == 0:
                    split_x(0, t // GROUP)
                split_w(t)
                if t == 5:
                    dve.wait_ge(assign_in, 32)
                    dve.wait_ge(cluster_id_ready, 2)
                    nc.vector.tensor_scalar(onehot[:, :], assign_bc, cluster_id[:, 0:1], None,
                                            ALU.is_equal).then_inc(onehot_ready, 1)
                if t == 7:
                    dve.wait_ge(logits_made, 1)
                    nc.vector.tensor_reduce(att_max, logit_ps, AX_X, ALU.max).then_inc(att_max_ready, 1)
                    dve.wait_ge(att_max_ready, 1)
                    nc.vector.tensor_scalar(att_neg, att_max, -1.0, None, ALU.mult).then_inc(att_neg_ready, 1)
                if t == 10:
                    dve.wait_ge(att_exp_ready, 1)
                    nc.vector.reciprocal(att_inv, att_sum).then_inc(att_inv_ready, 1)
                    dve.wait_ge(att_inv_ready, 1)
                    nc.vector.tensor_scalar(att, att_exp, att_inv, None, ALU.mult).then_inc(att_ready, 1)
                    dve.wait_ge(att_ready, 1)
                    dve.wait_ge(ident_ready, 1)
                    nc.vector.tensor_tensor(att_diag.rearrange("p (b k) -> p b k", k=K),
                                            ident.unsqueeze(2).broadcast_to([B, B, K]),
                                            att.unsqueeze(1).broadcast_to([B, B, K]),
                                            ALU.mult).then_inc(att_diag_ready, 1)
                if t == 13:
                    dve.wait_ge(att_spread, 1)
                    nc.vector.tensor_copy(att_bc[:, :], att_ps).then_inc(att_bc_ready, 1)
                    dve.wait_ge(att_bc_ready, 1)
                    dve.wait_ge(const_in, 32)
                    dve.wait_ge(onehot_ready, 1)
                    terms = temp[:, 0:B * K].rearrange("p (b k) -> p b k", k=K)
                    nc.vector.tensor_tensor(terms, att_bc[:, :].rearrange("p (b k) -> p b k", k=K),
                                            bkT[:, :].unsqueeze(1).broadcast_to([P, B, K]),
                                            ALU.mult).then_inc(agg_b_terms, 1)
                    dve.wait_ge(agg_b_terms, 1)
                    nc.vector.tensor_reduce(agg_b[:, :], terms, AX_X, ALU.add).then_inc(agg_b_ready, 1)
            dve.wait_ge(agg_b_ready, 1)
            mix_weights(0, 0, first=True)
            split_x(1, 0)
            copy_rowsum(0)
            for g in range(1, NG - 1):
                split_x(1, g)
            dve.wait_ge(rowsum_ready, 1)
            dve.wait_ge(bias_in, 16)
            dve.wait_ge(any_hit_zeroed, 1)

            def step_first(b, par):
                split_z(b - 1, 1 - par, 0)
                split_x(b, NG - 1)
                split_x(b + 1, 0)
                start_softmax(b - 1, 1 - par)
                finish_first(b - 1, 1 - par)
                find_hits(b - 1)
                split_x(b + 1, 1)
                mix_weights(b, b)
                split_x(b + 1, 2)

            step_first(1, 1)
            step_first(2, 0)
            with dve.Fori(0, B // 2 - 2) as pair:
                b = 2 * pair + 3
                step_first(b, 1)
                step_first(b + 1, 0)

            split_z(B - 2, 0, 0)
            split_x(B - 1, NG - 1)
            for g in range(NG - 1):
                split_x(B, g)
                for t in range(KT + g * GROUP, KT + (g + 1) * GROUP):
                    split_w(t)
                if g == 0:
                    start_softmax(B - 2, 0)
                    finish_first(B - 2, 0)
                    find_hits(B - 2)
                if g == 1:
                    mix_weights(B - 1, B - 1)

            split_z(B - 1, 1, 0)
            split_x(B, NG - 1)
            for t in range(2 * KT - GROUP, 2 * KT):
                split_w(t)
            split_x(B + 1, 0)
            start_softmax(B - 1, 1)
            finish_first(B - 1, 1)
            find_hits(B - 1)
            dve.wait_ge(hits_merged, B)
            nc.vector.tensor_copy(any_hit[:, 1, :], any_hit[:, 0, :]).then_inc(any_hit_doubled, 1)
            split_x(B + 1, 1)
            dve.wait_ge(counts_made, 1)
            nc.vector.tensor_scalar(sel_bc[:, :], z_ps[0][:, 2, 0:P], 0.5, None, ALU.is_gt).then_inc(sel_ready, 1)
            mix_weights(0, B)
            split_x(B + 1, 2)
            for c in range(4):
                dve.wait_ge(mask_made, c + 1)
                nc.vector.tensor_copy(row_mask[:, c * BANK:(c + 1) * BANK], z_ps[c % 2][:, 2, :]).then_inc(mask_ready, 1)
            copy_rowsum(1)
            dve.wait_ge(mask_ready, 4)
            dve.wait_ge(rowsum_ready, 2)
            dve.wait_ge(bias_in, 32)

            def step_second(b, par, last=False):
                s = b + B
                split_z(s - 1, 1 - par, 1)
                split_x(s, NG - 1)
                if not last:
                    split_x(s + 1, 0)
                finish_second(b - 1, s - 1, 1 - par)
                if not last:
                    split_x(s + 1, 1)
                mix_weights(b, s, outs=b)
                if not last:
                    split_x(s + 1, 2)

            step_second(1, 1)
            step_second(2, 0)
            with dve.Fori(0, B // 2 - 2) as pair:
                b = 2 * pair + 3
                step_second(b, 1)
                step_second(b + 1, 0)
            step_second(B - 1, 1, last=True)
            split_z(2 * B - 1, 1, 1)
            finish_second(B - 1, 2 * B - 1, 1)

        @block.tensor
        def _(pe):
            def group(s, par, phase, g, w_tile=None, small=None):
                pe.wait_ge(x_lo_ready, NG * s + g + 1)
                if g == 0 and (not isinstance(s, int) or s >= 2):
                    pe.wait_ge(z_lo_ready, s - 1)
                    if phase == 0:
                        pe.wait_ge(scores_ready, s - 1)
                for k in range(g * GROUP, (g + 1) * GROUP):
                    if w_tile is not None:
                        pe.wait_ge(w_lo_ready, w_tile + k + 1)
                    for xt, wt in ((x_hi, w_hi), (x_hi, w_lo), (x_lo, w_hi)):
                        for c, (a, e) in enumerate(CHUNKS[phase]):
                            last = nc.tensor.matmul(z_ps[par][:, c, 0:e - a], xt[:, k, :], wt[:, k, a:e],
                                                    start=(k == 0 and xt is x_hi and wt is w_hi),
                                                    stop=(k == KT - 1 and xt is x_lo))
                    if small is not None and k == (g + 1) * GROUP - 1:
                        last.then_inc(tiles_used, 1)
                        small(k)
                    elif k == (g + 1) * GROUP - 1:
                        last.then_inc(tiles_used, 1)
                    elif small is not None:
                        small(k)

            def mixed(dst, a, e):
                for n, (wt, zt) in enumerate(((agg_hi, z_hi), (agg_hi, z_lo), (agg_lo, z_hi))):
                    last = nc.tensor.matmul(dst, wt[:, :], zt[:, a:e], start=(n == 0), stop=(n == 2))
                return last

            def mix(s, par, phase):
                pe.wait_ge(agg_ready, s + 1)
                pe.wait_ge(z_lo_ready, s + 1)
                if phase == 0:
                    mixed(z_ps[par][:, 2, DOTS_AT:DOTS_AT + NC], HALF, WIDE).then_inc(dots_ready, 1)
                for c in range(2):
                    last = mixed(d_ps[:, c, :], c * BANK, (c + 1) * BANK)
                last.then_inc(dense_ready, 1)

            def sum_rows(phase):
                pe.wait_ge(w_summed, KT * (phase + 1))
                for c in range(2):
                    last = nc.tensor.matmul(d_ps[:, c, :], ones[:, :], w_sum[:, c * BANK:(c + 1) * BANK],
                                            start=True, stop=True)
                if phase == 0:
                    last = nc.tensor.matmul(z_ps[1][:, 2, 0:NC], ones[:, :], w_sum[:, HALF:WIDE],
                                            start=True, stop=True)
                last.then_inc(rowsum_made, 1)

            def small(k):
                if k == 0:
                    pe.wait_ge(cond_in, 16 * 7)
                    nc.tensor.matmul(h1_ps, w0_sb, cond_sb, start=True, stop=True).then_inc(h1_made, 1)
                if k == 3:
                    pe.wait_ge(h1_ready, 1)
                    nc.tensor.matmul(h2_ps, w1_sb, h1, start=True, stop=True).then_inc(h2_made, 1)
                if k == 6:
                    pe.wait_ge(h2_ready, 1)
                    pe.wait_ge(ones_ready, 1)
                    nc.tensor.matmul(logit_ps, h2, w2_sb, start=True, stop=False)
                    nc.tensor.matmul(logit_ps, ones[0:1, 0:B], b2_sb, start=False, stop=True).then_inc(logits_made, 1)
                if k == 12:
                    pe.wait_ge(att_diag_ready, 1)
                    nc.tensor.matmul(att_ps, ones[0:B, :], att_diag, start=True, stop=True).then_inc(att_spread, 1)

            for g in range(NG):
                group(0, 0, 0, g, w_tile=0, small=small)
            pe.wait_ge(att_bc_ready, 1)
            sum_rows(0)

            def step_first(b, par):
                group(b, par, 0, 0)
                pe.wait_ge(rowsum_ready, 1)
                if not isinstance(b, int) or b >= 2:
                    pe.wait_ge(half_ready, b - 1)
                mix(b - 1, 1 - par, 0)
                for g in range(1, NG):
                    group(b, par, 0, g)

            pe.wait_ge(cluster_sum_ready, 1)
            step_first(1, 1)
            step_first(2, 0)
            with pe.Fori(0, B // 2 - 2) as pair:
                b = 2 * pair + 3
                step_first(b, 1)
                step_first(b + 1, 0)
            step_first(B - 1, 1)

            group(B, 0, 1, 0, w_tile=KT)
            pe.wait_ge(half_ready, B - 1)
            mix(B - 1, 1, 0)
            group(B, 0, 1, 1, w_tile=KT)
            pe.wait_ge(any_hit_doubled, 1)
            nc.tensor.matmul(z_ps[0][:, 2, 0:P], any_hit[:, :, :].rearrange("p a n -> p (a n)"), ones[:, :],
                             start=True, stop=True).then_inc(counts_made, 1)
            for c in range(4):
                if c % 2 == 0:
                    group(B, 0, 1, 2 + c // 2, w_tile=KT)
                if c == 0:
                    pe.wait_ge(sel_ready, 1)
                if c >= 2:
                    pe.wait_ge(mask_ready, c - 1)
                half = c // 2
                rows = slice(half * NC, (half + 1) * NC)
                nc.tensor.matmul(z_ps[c % 2][:, 2, :], sel_bc[rows, :], onehot[rows, (c % 2) * BANK:(c % 2 + 1) * BANK],
                                 start=True, stop=True).then_inc(mask_made, 1)
            pe.wait_ge(half_ready, B)
            sum_rows(1)

            def step_second(b, par):
                group(b + B, par, 1, 0)
                pe.wait_ge(rowsum_ready, 2)
                if not isinstance(b, int) or b >= 2:
                    pe.wait_ge(dense_drained, b - 1)
                mix(b + (B - 1), 1 - par, 1)
                for g in range(1, NG):
                    group(b + B, par, 1, g)

            step_second(1, 1)
            step_second(2, 0)
            with pe.Fori(0, B // 2 - 2) as pair:
                b = 2 * pair + 3
                step_second(b, 1)
                step_second(b + 1, 0)
            step_second(B - 1, 1)
            pe.wait_ge(dense_drained, B - 1)
            mix(2 * B - 1, 1, 1)


def kernel(**inputs):
    import concourse.bacc as bacc
    from concourse.bass_utils import run_bass_kernel_spmd

    x = np.ascontiguousarray(inputs["x"])
    B, T, H = x.shape
    kt, half = H // P, H // 2
    weight_T = np.asarray(inputs["L0_ffn_weight"]).T.reshape(kt, P, H)
    centroids_T = np.asarray(inputs["L0_ffn_centroids"]).T.reshape(kt, P, -1)
    arrays = {
        "x": x,
        "xT": x.transpose(0, 2, 1).reshape(B, kt, P, T).transpose(0, 2, 1, 3),
        "w_first": np.concatenate([weight_T[:, :, :half], centroids_T], axis=2),
        "w_second": weight_T[:, :, half:],
        "cond_T": np.asarray(inputs["cond_128"]).T,
        "W0": inputs["L0_cond_W0"],
        "b0": inputs["L0_cond_b0"],
        "W1": inputs["L0_cond_W1"],
        "b1": inputs["L0_cond_b1"],
        "W2": inputs["L0_cond_W2"],
        "b2": inputs["L0_cond_b2"],
        "wk_T": np.asarray(inputs["L0_cond_weight"])[..., 0].transpose(2, 1, 0),
        "bias_k_T": np.asarray(inputs["L0_cond_bias_k"]).T,
        "ffn_bias": inputs["L0_ffn_bias"],
        "assignments": inputs["L0_ffn_assignments"],
    }
    nc = bacc.Bacc("TRN2", target_bir_lowering=False, num_devices=1, dynamic_dma_scratch_size=1024)
    feed, args = {}, []
    for name, a in arrays.items():
        feed[f"in_{name}"] = np.ascontiguousarray(a)
        a = feed[f"in_{name}"]
        args.append(nc.dram_tensor(f"in_{name}", a.shape, mybir.dt.from_np(a.dtype), kind="ExternalInput").ap())
    args.append(nc.dram_tensor("out", x.shape, F32, kind="ExternalOutput").ap())
    adaln_ffn_kernel(nc, *args)
    r = run_bass_kernel_spmd(nc, [feed], core_ids=[0])
    return r.results[0]["out"]
```

```python
from contextlib import ExitStack

import numpy as np

import concourse.bass as bass
from concourse import mybir

ALU = mybir.AluOpType
ACT = mybir.ActivationFunctionType
F32 = mybir.dt.float32
F32R = mybir.dt.float32r
BF16 = mybir.dt.bfloat16
I32 = mybir.dt.int32
U8 = mybir.dt.uint8
AX_X = mybir.AxisListType.X

P = 128
BANK = 512
GROUP = 4
THRESHOLD = 0.01
INV_TEMPERATURE = 10.0



def adaln_ffn_kernel(nc, x, xT, w_first, w_second, small_in, wk_T, ffn_bias, assignments, out):
    B, _, H = x.shape
    KT = H // P
    HALF = H // 2
    NC = w_first.shape[2] - HALF
    WIDE = HALF + NC
    NG = KT // GROUP
    K = wk_T.shape[2]
    WSLOTS = 4
    SUMMED = [t for t in range(KT) if t % 8 in (0, 2, 3, 5, 7)]
    TAIL = [(0, BANK), (BANK, BANK + 256), (BANK + 256, HALF)]

    CHUNKS = [[(0, 384), (384, 768), (768, WIDE)], [(0, BANK), (BANK, HALF)]]
    DOTS_AT = CHUNKS[0][2][1] - CHUNKS[0][2][0]
    assert DOTS_AT + NC <= BANK and KT % GROUP == 0 and B % 2 == 0

    with ExitStack() as ctx:
        def sb(name, shape, dt):
            return ctx.enter_context(nc.sbuf_tensor(name, shape, dt))

        def sem(name):
            return ctx.enter_context(nc.semaphore(name))

        w_hi = sb("w_hi", [P, KT, WIDE], F32R)
        w_lo = sb("w_lo", [P, KT, WIDE], F32R)
        x_hi = sb("x_hi", [P, KT, P], F32R)
        x_lo = sb("x_lo", [P, KT, P], F32R)
        x_raw = sb("x_raw", [P, KT, P], F32)
        stage = sb("stage", [P, WSLOTS * WIDE], F32)
        z_hi = sb("z_hi", [P, WIDE], F32R)
        z_lo = sb("z_lo", [P, WIDE], F32R)
        w_sum = sb("w_sum", [P, WIDE], F32)
        rowsum = sb("rowsum", [P, WIDE], F32)
        bias_bc = sb("bias_bc", [P, HALF], F32)
        row_mask = sb("row_mask", [P, H], U8)
        temp = sb("temp", [P, HALF], F32)
        first_half = sb("first_half", [P, 2, HALF], F32)
        wk = sb("wk", [P, P, K], F32)
        onehot = sb("onehot", [P, HALF], BF16)
        att_bc = sb("att_bc", [P, B * K], F32)
        agg_b = sb("agg_b", [P, B], F32)
        agg_w = sb("agg_w", [P, P], F32)
        agg_hi = sb("agg_hi", [P, P], F32R)
        agg_lo = sb("agg_lo", [P, P], F32R)
        scores = sb("scores", [P, NC], F32)
        probs = sb("probs", [P, NC], F32)
        any_hit = sb("any_hit", [P, 2, NC], F32)
        sel_bc = sb("sel_bc", [P, P], BF16)
        query_sel = sb("query_sel", [P, B], F32)
        row_max = sb("row_max", [P, 1], F32)
        neg_max = sb("neg_max", [P, 1], F32)
        exp_sum = sb("exp_sum", [P, 1], F32)
        exp_inv = sb("exp_inv", [P, 1], F32)
        ones_r = sb("ones_r", [P, P], F32R)
        ones = ones_r[:, :].bitcast(F32)
        cluster_id = sb("cluster_id", [P, 1], F32)

        early = first_half[:, :, :].rearrange("p a n -> p (a n)")
        cut = {}
        at = 0
        for name, width in small_columns(P, B, K):
            cut[name] = early[:, at:at + width]
            at += width
        packed = early[:, 0:at]
        w0_sb, w1_sb, w2_sb, cond_sb = cut["W0"], cut["W1"], cut["W2"], cut["cond_T"]
        b0_sb, b1_sb, b2_sb, bkT = cut["b0"], cut["b1"], cut["b2"][0:1, :], cut["bias_k_T"]
        h1 = early[:, 384:384 + B]
        h2 = early[:, 416:416 + B]
        ident = early[0:B, 448:448 + B]
        att_max = early[0:B, 480:481]
        att_neg = early[0:B, 481:482]
        att_sum = early[0:B, 482:483]
        att_inv = early[0:B, 483:484]
        att_exp = early[0:B, 484:484 + K]
        att = early[0:B, 492:492 + K]
        att_diag = early[0:B, 512:512 + B * K]
        agg_b_term = early[:, 768:768 + B * K]
        assign_bc = first_half[:, 1, :].bitcast(I32)

        z_ps = [ctx.enter_context(nc.psum_tensor(f"z_ps{i}", [P, 3, BANK], F32)) for i in range(2)]
        d_ps = ctx.enter_context(nc.psum_tensor("d_ps", [P, 2, BANK], F32))
        h1_ps, h2_ps = z_ps[1][:, 0, 0:B], z_ps[1][:, 0, B:2 * B]
        logit_ps = z_ps[1][0:B, 0, 2 * B:2 * B + K]
        att_ps = z_ps[1][:, 1, 0:B * K]

        dram_half = nc.dram_tensor("dense_first_half", [B, P, HALF], F32, kind="Internal").ap()

        x_start_in = [sem(f"x_start_in{g}") for g in range(KT // GROUP)]
        x_raw_in = sem("x_raw_in")
        w_raw_in = [sem(f"w_raw_in{i}") for i in range(WSLOTS)]
        small_done = sem("small_done")
        bias_in = sem("bias_in")
        wk_in = sem("wk_in")
        assign_in = sem("assign_in")
        half_out = [sem(f"half_out{i}") for i in range(2)]
        rest_in = [sem(f"rest_in{i}") for i in range(2)]
        out_done = [sem(f"out_done{i}") for i in range(2)]
        ones_ready = sem("ones_ready")
        zero_ready = sem("zero_ready")
        ident_ready = sem("ident_ready")
        cluster_id_ready = sem("cluster_id_ready")
        onehot_ready = sem("onehot_ready")
        any_hit_zeroed = sem("any_hit_zeroed")
        w_hi_ready = sem("w_hi_ready")
        w_lo_ready = sem("w_lo_ready")
        w_summed = sem("w_summed")
        sum_raw_in = sem("sum_raw_in")
        x_hi_ready = sem("x_hi_ready")
        x_lo_ready = sem("x_lo_ready")
        z_hi_ready = sem("z_hi_ready")
        z_lo_ready = sem("z_lo_ready")
        tiles_used = sem("tiles_used")
        dots_ready = sem("dots_ready")
        dense_ready = sem("dense_ready")
        dense_drained = sem("dense_drained")
        rowsum_made = sem("rowsum_made")
        cluster_sum_ready = sem("cluster_sum_ready")
        rowsum_ready = sem("rowsum_ready")
        h1_made = sem("h1_made")
        h1_ready = sem("h1_ready")
        h2_made = sem("h2_made")
        h2_ready = sem("h2_ready")
        logits_made = sem("logits_made")
        att_max_ready = sem("att_max_ready")
        att_neg_ready = sem("att_neg_ready")
        att_exp_ready = sem("att_exp_ready")
        att_inv_ready = sem("att_inv_ready")
        att_ready = sem("att_ready")
        att_diag_ready = sem("att_diag_ready")
        att_spread = sem("att_spread")
        att_bc_ready = sem("att_bc_ready")
        agg_b_terms = sem("agg_b_terms")
        agg_b_ready = sem("agg_b_ready")
        agg_terms = sem("agg_terms")
        agg_summed = sem("agg_summed")
        agg_hi_ready = sem("agg_hi_ready")
        agg_ready = sem("agg_ready")
        scores_ready = sem("scores_ready")
        row_max_ready = sem("row_max_ready")
        neg_max_ready = sem("neg_max_ready")
        probs_ready = sem("probs_ready")
        exp_inv_ready = sem("exp_inv_ready")
        hit_ready = sem("hit_ready")
        hits_merged = sem("hits_merged")
        any_hit_doubled = sem("any_hit_doubled")
        counts_made = sem("counts_made")
        sel_ready = sem("sel_ready")
        mask_made = sem("mask_made")
        mask_ready = sem("mask_ready")
        offset_ready = sem("offset_ready")
        half_ready = sem("half_ready")
        masked_ready = sem("masked_ready")
        half_masked = sem("half_masked")
        out_ready = sem("out_ready")
        tail_z = sem("tail_z")
        tail_hi = sem("tail_hi")
        tail_lo = sem("tail_lo")
        tail_dense = sem("tail_dense")
        tail_masked_offset = sem("tail_masked_offset")
        tail_scale = sem("tail_scale")
        tail_half_masked = sem("tail_half_masked")
        tail_half_ready = sem("tail_half_ready")
        tail_base = sem("tail_base")
        tail_scaled = sem("tail_scaled")
        tail_ready = sem("tail_ready")
        tail_out = sem("tail_out")

        def slot(t, width):
            return stage[:, (t % WSLOTS) * WIDE:(t % WSLOTS) * WIDE + width]

        def rest(par):
            return stage[:, par * H:(par + 1) * H]

        def width_of(t):
            return WIDE if t < KT else HALF

        def xg(t, g):
            return t[:, g * GROUP:(g + 1) * GROUP, :]

        def turn(b, par):
            return 8 * b + (8 if par else 16)

        block = ctx.enter_context(nc.Block())

        @block.sync
        def _(sp):
            def load_x(b, s):
                sp.wait_ge(x_lo_ready, NG * s)
                sp.dma_start(x_raw[:, :, :], xT[b, :, :, :]).then_inc(x_raw_in, 16)

            def load_w(t):
                if t >= WSLOTS and t != KT:
                    sp.wait_ge(w_lo_ready, t - WSLOTS + 1)
                if WSLOTS <= t < KT and t - WSLOTS in SUMMED:
                    sp.wait_ge(w_summed, SUMMED.index(t - WSLOTS) + 1)
                src = w_first[t, :, :] if t < KT else w_second[t - KT, :, :]
                sp.dma_start(slot(t, width_of(t)), src).then_inc(w_raw_in[t % WSLOTS], 16)

            def load_for_sum(n):
                sp.wait_ge(w_summed, n + len(SUMMED))
                sp.dma_start(slot(0, HALF), w_second[n, :, :]).then_inc(sum_raw_in, 16)

            def store_half(b, par):
                sp.wait_ge(half_ready, b + 1)
                sp.dma_start(dram_half[b, :, :], first_half[:, par, :]).then_inc(half_out[par], 16)

            def load_rest(b, par):
                sp.dma_start(rest(par), x[b, :, :]).then_inc(rest_in[par], 16)
                sp.dma_start(first_half[:, par, :], dram_half[b, :, :]).then_inc(rest_in[par], 16)

            def store_out(b, par):
                sp.wait_ge(out_ready, b + 1)
                sp.dma_start(out[b, :, :], rest(par)).then_inc(out_done[par], 16)

            for t in range(KT):
                if t % GROUP == 0:
                    g = t // GROUP
                    sp.dma_start(xg(x_raw, g), xg(xT[0], g)).then_inc(x_start_in[g], 16)
                load_w(t)
                if t == 0:
                    sp.dma_start(packed, small_in).then_inc(small_done, 16)
            sp.dma_start(wk[:, :, :], wk_T).then_inc(wk_in, 16)
            load_x(1, 1)
            sp.dma_start(bias_bc[:, :], ffn_bias[0:HALF].partition_broadcast(P)).then_inc(bias_in, 16)
            for g in range(2):
                sp.dma_start(assign_bc[g * NC:(g + 1) * NC, :],
                             assignments[g * HALF:(g + 1) * HALF].partition_broadcast(NC)).then_inc(assign_in, 16)
            sp.wait_ge(w_lo_ready, KT)

            def step_first(b, par):
                load_x(b + 1, b + 1)
                store_half(b - 1, 1 - par)

            step_first(1, 1)
            load_for_sum(0)
            step_first(2, 0)
            load_for_sum(1)
            with sp.Fori(0, B // 2 - 2) as pair:
                b = 2 * pair + 3
                step_first(b, 1)
                load_for_sum(pair + 2)
                step_first(b + 1, 0)
            sp.wait_ge(w_summed, len(SUMMED) + KT)
            for t in range(KT, KT + GROUP):
                load_w(t)
            load_x(0, B)
            for t in range(KT + GROUP, KT + 2 * GROUP):
                load_w(t)
            store_half(B - 2, 0)
            for t in range(KT + 2 * GROUP, 2 * KT):
                load_w(t)
            load_x(1, B + 1)
            store_half(B - 1, 1)
            sp.wait_ge(offset_ready, B)
            sp.dma_start(bias_bc[:, :], ffn_bias[HALF:H].partition_broadcast(P)).then_inc(bias_in, 16)
            sp.wait_ge(w_lo_ready, 2 * KT)
            for par in range(2):
                sp.wait_ge(half_out[par], turn(B - 2 + par, par))
            load_rest(0, 0)

            def step_second(b, par):
                load_x(b + 1, B + b + 1)
                if not isinstance(b, int) or b >= 2:
                    sp.wait_ge(out_done[par], turn(b, par) - 16)
                load_rest(b, par)
                store_out(b - 1, 1 - par)

            step_second(1, 1)
            step_second(2, 0)
            with sp.Fori(0, B // 2 - 2) as pair:
                b = 2 * pair + 3
                step_second(b, 1)
                step_second(b + 1, 0)
            sp.wait_ge(out_done[1], turn(B - 3, 1))
            load_rest(B - 1, 1)
            store_out(B - 2, 0)
            sp.wait_ge(tail_half_ready, 1)
            sp.dma_start(out[B - 1, :, 0:HALF], rest(1)[:, 0:HALF]).then_inc(tail_out, 16)
            for c, (a, e) in enumerate(TAIL):
                sp.wait_ge(tail_ready, c + 1)
                sp.dma_start(out[B - 1, :, HALF + a:HALF + e], rest(1)[:, HALF + a:HALF + e]).then_inc(tail_out, 16)
            sp.wait_ge(out_done[0], turn(B - 2, 0))
            sp.wait_ge(out_done[1], turn(B - 3, 1))
            sp.wait_ge(tail_out, 16 * (1 + len(TAIL)))

        @block.gpsimd
        def _(pool):
            nc.gpsimd.memset(ones, 1.0).then_inc(ones_ready, 1)
            nc.gpsimd.memset(ident, 0.0).then_inc(zero_ready, 1)
            pool.wait_ge(zero_ready, 1)
            nc.gpsimd.affine_select(out=ident, in_=ident, compare_op=ALU.not_equal, fill=1.0, base=0,
                                    pattern=[[-1, B]], channel_multiplier=1).then_inc(ident_ready, 1)
            for g in range(2):
                pool.wait_ge(ident_ready, 1)
                if g:
                    pool.wait_ge(cluster_id_ready, g)
                nc.gpsimd.iota(cluster_id[g * NC:(g + 1) * NC, :], [[0, 1]], base=0, channel_multiplier=1,
                               allow_small_or_imprecise_dtypes=True).then_inc(cluster_id_ready, 1)
            pool.wait_ge(ones_ready, 1)
            pool.wait_ge(cluster_id_ready, 2)
            for n, t in enumerate(SUMMED):
                pool.wait_ge(w_raw_in[t % WSLOTS], 16 * (t // WSLOTS + 1))
                if n == 0:
                    nc.gpsimd.tensor_copy(w_sum[:, :], slot(t, WIDE)).then_inc(w_summed, 1)
                else:
                    pool.wait_ge(w_summed, n)
                    nc.gpsimd.tensor_tensor(w_sum[:, :], w_sum[:, :], slot(t, WIDE), ALU.add).then_inc(w_summed, 1)

            def add_tile(n):
                pool.wait_ge(w_summed, n + len(SUMMED))
                pool.wait_ge(sum_raw_in, 16 * n + 16)
                nc.gpsimd.tensor_tensor(w_sum[:, 0:HALF], w_sum[:, 0:HALF], slot(0, HALF), ALU.add).then_inc(w_summed, 1)

            pool.wait_ge(rowsum_made, 1)
            pool.wait_ge(sum_raw_in, 16)
            nc.gpsimd.tensor_copy(w_sum[:, 0:HALF], slot(0, HALF)).then_inc(w_summed, 1)
            add_tile(1)
            with pool.Fori(0, B // 2 - 2) as pair:
                add_tile(pair + 2)

        @block.scalar
        def _(act):
            def split_w(t):
                width = width_of(t)
                act.wait_ge(w_raw_in[t % WSLOTS], 16 * (t // WSLOTS + 1))
                if t >= KT and t % GROUP == 0:
                    act.wait_ge(tiles_used, NG * (B - 1) + (t - KT) // GROUP + 1)
                nc.scalar.copy(w_hi[:, t % KT, 0:width], slot(t, width)).then_inc(w_hi_ready, 1)

            def split_x(s, g):
                act.wait_ge(x_raw_in, 16 * s)
                act.wait_ge(tiles_used, NG * s - NG + g + 1)
                nc.scalar.copy(xg(x_hi, g), xg(x_raw, g)).then_inc(x_hi_ready, 1)

            def split_z(s, par, phase, wait_before=True):
                act.wait_ge(tiles_used, NG * s + NG)
                if wait_before:
                    act.wait_ge(dense_ready, s)
                if phase == 0:
                    nc.scalar.copy(z_hi[:, 0:768].rearrange("p (a n) -> p a n", a=2), z_ps[par][:, 0:2, 0:384])
                    nc.scalar.copy(z_hi[:, 768:WIDE], z_ps[par][:, 2, 0:WIDE - 768]).then_inc(z_hi_ready, 1)
                else:
                    nc.scalar.copy(z_hi[:, 0:HALF].rearrange("p (a n) -> p a n", a=2),
                                   z_ps[par][:, 0:2, :]).then_inc(z_hi_ready, 1)

            def exp_scores(s):
                act.wait_ge(neg_max_ready, s + 1)
                nc.scalar.activation(probs[:, :], scores[:, :], ACT.Exp, bias=neg_max[:, :],
                                     scale=INV_TEMPERATURE, accum_out=exp_sum[:, :]).then_inc(probs_ready, 1)

            for t in range(KT):
                if t % GROUP == 0:
                    act.wait_ge(x_start_in[t // GROUP], 16)
                    nc.scalar.copy(xg(x_hi, t // GROUP), xg(x_raw, t // GROUP)).then_inc(x_hi_ready, 1)
                split_w(t)
                if t == 2:
                    act.wait_ge(h1_made, 1)
                    act.wait_ge(small_done, 16)
                    nc.scalar.activation(h1, h1_ps, ACT.Gelu, bias=b0_sb).then_inc(h1_ready, 1)
                if t == 4:
                    act.wait_ge(h2_made, 1)
                    nc.scalar.activation(h2, h2_ps, ACT.Gelu, bias=b1_sb).then_inc(h2_ready, 1)
                if t == 8:
                    act.wait_ge(att_neg_ready, 1)
                    nc.scalar.activation(att_exp, logit_ps, ACT.Exp, bias=att_neg,
                                         accum_out=att_sum).then_inc(att_exp_ready, 1)
            for g in range(NG - 1):
                split_x(1, g)

            def step(b, s, par, phase, last=False):
                split_z(s - 1, 1 - par, phase)
                split_x(s, NG - 1)
                if not last:
                    split_x(s + 1, 0)
                if phase == 0:
                    exp_scores(s - 1)
                for g in range(1, NG - 1):
                    if not last:
                        split_x(s + 1, g)

            step(1, 1, 1, 0)
            step(2, 2, 0, 0)
            with act.Fori(0, B // 2 - 2) as pair:
                b = 2 * pair + 3
                step(b, b, 1, 0)
                step(b + 1, b + 1, 0, 0)
            split_z(B - 2, 0, 0)
            split_x(B - 1, NG - 1)
            for g in range(NG - 1):
                split_x(B, g)
                for t in range(KT + g * GROUP, KT + (g + 1) * GROUP):
                    split_w(t)
                if g == 0:
                    exp_scores(B - 2)
            split_z(B - 1, 1, 0)
            split_x(B, NG - 1)
            for t in range(2 * KT - GROUP, 2 * KT):
                split_w(t)
            split_x(B + 1, 0)
            exp_scores(B - 1)
            for g in range(1, NG - 1):
                split_x(B + 1, g)
            step(1, B + 1, 1, 1)
            step(2, B + 2, 0, 1)
            with act.Fori(0, B // 2 - 2) as pair:
                b = 2 * pair + 3
                step(b, b + B, 1, 1)
                step(b + 1, b + (B + 1), 0, 1)
            step(B - 1, 2 * B - 1, 1, 1, last=True)
            act.wait_ge(dense_ready, 2 * B - 1)
            for c, (a, e) in enumerate(TAIL):
                act.wait_ge(tail_z, c + 1)
                nc.scalar.copy(z_hi[:, a:e], z_ps[1][:, c, 0:e - a]).then_inc(tail_hi, 1)

        @block.vector
        def _(dve):
            def split_w(t):
                width = width_of(t)
                dve.wait_ge(w_hi_ready, t + 1)
                nc.vector.tensor_tensor(w_lo[:, t % KT, 0:width], slot(t, width),
                                        w_hi[:, t % KT, 0:width].bitcast(F32), ALU.subtract).then_inc(w_lo_ready, 1)

            def split_x(s, g):
                dve.wait_ge(x_hi_ready, NG * s + g + 1)
                nc.vector.tensor_tensor(xg(x_lo, g), xg(x_raw, g), xg(x_hi, g).bitcast(F32),
                                        ALU.subtract).then_inc(x_lo_ready, 1)

            def split_z(s, par, phase):
                dve.wait_ge(z_hi_ready, s + 1)
                if phase == 0:
                    nc.vector.tensor_tensor(z_lo[:, 0:768].rearrange("p (a n) -> p a n", a=2),
                                            z_ps[par][:, 0:2, 0:384],
                                            z_hi[:, 0:768].bitcast(F32).rearrange("p (a n) -> p a n", a=2),
                                            ALU.subtract)
                    nc.vector.tensor_tensor(z_lo[:, 768:WIDE], z_ps[par][:, 2, 0:WIDE - 768],
                                            z_hi[:, 768:WIDE].bitcast(F32), ALU.subtract).then_inc(z_lo_ready, 1)
                else:
                    nc.vector.tensor_tensor(z_lo[:, 0:HALF].rearrange("p (a n) -> p a n", a=2),
                                            z_ps[par][:, 0:2, :],
                                            z_hi[:, 0:HALF].bitcast(F32).rearrange("p (a n) -> p a n", a=2),
                                            ALU.subtract).then_inc(z_lo_ready, 1)

            def sum_experts(b, s, scratch):
                terms = scratch[:, 0:P * K].rearrange("p (o k) -> p o k", k=K)
                att_b = att_bc[:, bass.ds(b * K, K)].unsqueeze(1).broadcast_to([P, P, K])
                nc.vector.tensor_tensor(terms, wk[:, :, :], att_b, ALU.mult).then_inc(agg_terms, 1)
                dve.wait_ge(agg_terms, s + 1)
                if not isinstance(s, int) or s > 0:
                    dve.wait_ge(agg_ready, s)
                nc.vector.tensor_reduce(agg_w[:, :], terms, AX_X, ALU.add).then_inc(agg_summed, 1)

            def split_agg(s):
                dve.wait_ge(agg_summed, s + 1)
                if not isinstance(s, int) or s > 0:
                    dve.wait_ge(dense_ready, s)
                nc.vector.tensor_copy(agg_hi[:, :], agg_w[:, :]).then_inc(agg_hi_ready, 1)
                dve.wait_ge(agg_hi_ready, s + 1)
                nc.vector.tensor_tensor(agg_lo[:, :], agg_w[:, :], agg_hi[:, :].bitcast(F32),
                                        ALU.subtract).then_inc(agg_ready, 1)

            def mix_weights(b, s):
                sum_experts(b, s, temp)
                split_agg(s)

            def start_softmax(b, par):
                dve.wait_ge(dots_ready, b + 1)
                nc.vector.scalar_tensor_tensor(out=scores[:, :], in0=rowsum[:, HALF:WIDE],
                                               scalar=agg_b[:, bass.ds(b, 1)],
                                               in1=z_ps[par][:, 2, DOTS_AT:DOTS_AT + NC],
                                               op0=ALU.mult, op1=ALU.add).then_inc(scores_ready, 1)
                dve.wait_ge(scores_ready, b + 1)
                nc.vector.tensor_reduce(row_max[:, :], scores[:, :], AX_X, ALU.max).then_inc(row_max_ready, 1)
                dve.wait_ge(row_max_ready, b + 1)
                nc.vector.tensor_scalar(neg_max[:, :], row_max[:, :], -INV_TEMPERATURE, None,
                                        ALU.mult).then_inc(neg_max_ready, 1)

            def find_hits(b):
                dve.wait_ge(probs_ready, b + 1)
                nc.vector.reciprocal(exp_inv[:, :], exp_sum[:, :]).then_inc(exp_inv_ready, 1)
                dve.wait_ge(exp_inv_ready, b + 1)
                nc.vector.tensor_scalar(probs[:, :], probs[:, :], exp_inv[:, 0:1], THRESHOLD,
                                        ALU.mult, ALU.is_gt).then_inc(hit_ready, 1)
                dve.wait_ge(hit_ready, b + 1)
                nc.vector.tensor_reduce(query_sel[:, bass.ds(b, 1)], probs[:, :], AX_X, ALU.max)
                nc.vector.tensor_tensor(any_hit[:, 0, :], any_hit[:, 0, :], probs[:, :],
                                        ALU.max).then_inc(hits_merged, 1)

            def make_offset(dst, b, s):
                nc.vector.scalar_tensor_tensor(out=dst, in0=rowsum[:, 0:HALF], scalar=agg_b[:, bass.ds(b, 1)],
                                               in1=bias_bc[:, :], op0=ALU.mult, op1=ALU.add).then_inc(offset_ready, 1)
                dve.wait_ge(offset_ready, s + 1)

            def dense_of(dst, s, ready):
                dve.wait_ge(dense_ready, s + 1)
                nc.vector.tensor_tensor(dst, dst, d_ps[:, :, :].rearrange("p a n -> p (a n)"),
                                        ALU.add).then_inc(ready, 1)

            def finish_first(b, par):
                if not isinstance(b, int) or b >= 2:
                    dve.wait_ge(half_out[par], turn(b, par) - 16)
                make_offset(first_half[:, par, :], b, b)
                dense_of(first_half[:, par, :], b, half_ready)

            def finish_second(b, s, par):
                rows = rest(par)
                dense_of(temp[:, :], s, dense_drained)
                dve.wait_ge(dense_drained, b + 1)
                nc.vector.scalar_tensor_tensor(out=temp[:, :], in0=temp[:, :], scalar=query_sel[:, bass.ds(b, 1)],
                                               in1=row_mask[:, HALF:H], op0=ALU.mult,
                                               op1=ALU.mult).then_inc(masked_ready, 1)
                dve.wait_ge(rest_in[par], 2 * turn(b, par))
                nc.vector.scalar_tensor_tensor(out=first_half[:, par, :], in0=first_half[:, par, :],
                                               scalar=query_sel[:, bass.ds(b, 1)], in1=row_mask[:, 0:HALF],
                                               op0=ALU.mult, op1=ALU.mult).then_inc(half_masked, 1)
                dve.wait_ge(half_masked, b + 1)
                nc.vector.tensor_tensor(rows[:, 0:HALF], rows[:, 0:HALF], first_half[:, par, :], ALU.add)
                dve.wait_ge(masked_ready, b + 1)
                nc.vector.tensor_tensor(rows[:, HALF:H], rows[:, HALF:H], temp[:, :], ALU.add).then_inc(out_ready, 1)

            def copy_rowsum(phase):
                dve.wait_ge(rowsum_made, phase + 1)
                if phase == 0:
                    nc.vector.tensor_copy(rowsum[:, HALF:WIDE], z_ps[1][:, 2, 0:NC]).then_inc(cluster_sum_ready, 1)
                nc.vector.tensor_copy(rowsum[:, 0:HALF],
                                      d_ps[:, :, :].rearrange("p a n -> p (a n)")).then_inc(rowsum_ready, 1)

            nc.vector.memset(any_hit[:, :, :], 0.0).then_inc(any_hit_zeroed, 1)
            for t in range(KT):
                if t % GROUP == 0:
                    split_x(0, t // GROUP)
                split_w(t)
                if t == 7:
                    dve.wait_ge(logits_made, 1)
                    nc.vector.tensor_reduce(att_max, logit_ps, AX_X, ALU.max).then_inc(att_max_ready, 1)
                    dve.wait_ge(att_max_ready, 1)
                    nc.vector.tensor_scalar(att_neg, att_max, -1.0, None, ALU.mult).then_inc(att_neg_ready, 1)
                if t == 10:
                    dve.wait_ge(att_exp_ready, 1)
                    nc.vector.reciprocal(att_inv, att_sum).then_inc(att_inv_ready, 1)
                    dve.wait_ge(att_inv_ready, 1)
                    nc.vector.tensor_scalar(att, att_exp, att_inv, None, ALU.mult).then_inc(att_ready, 1)
                    dve.wait_ge(att_ready, 1)
                    dve.wait_ge(ident_ready, 1)
                    nc.vector.tensor_tensor(att_diag.rearrange("p (b k) -> p b k", k=K),
                                            ident.unsqueeze(2).broadcast_to([B, B, K]),
                                            att.unsqueeze(1).broadcast_to([B, B, K]),
                                            ALU.mult).then_inc(att_diag_ready, 1)
                if t == 13:
                    dve.wait_ge(att_spread, 1)
                    nc.vector.tensor_copy(att_bc[:, :], att_ps).then_inc(att_bc_ready, 1)
                    dve.wait_ge(att_bc_ready, 1)
                    terms = agg_b_term.rearrange("p (b k) -> p b k", k=K)
                    nc.vector.tensor_tensor(terms, att_bc[:, :].rearrange("p (b k) -> p b k", k=K),
                                            bkT.unsqueeze(1).broadcast_to([P, B, K]),
                                            ALU.mult).then_inc(agg_b_terms, 1)
                    dve.wait_ge(agg_b_terms, 1)
                    nc.vector.tensor_reduce(agg_b[:, :], terms, AX_X, ALU.add).then_inc(agg_b_ready, 1)
            dve.wait_ge(agg_b_ready, 1)
            dve.wait_ge(wk_in, 16)
            mix_weights(0, 0)
            split_x(1, 0)
            copy_rowsum(0)
            for g in range(1, NG - 1):
                split_x(1, g)
            dve.wait_ge(assign_in, 32)
            dve.wait_ge(cluster_id_ready, 2)
            nc.vector.tensor_scalar(onehot[:, :], assign_bc, cluster_id[:, 0:1], None,
                                    ALU.is_equal).then_inc(onehot_ready, 1)
            dve.wait_ge(onehot_ready, 1)
            dve.wait_ge(rowsum_ready, 1)
            dve.wait_ge(bias_in, 16)
            dve.wait_ge(any_hit_zeroed, 1)

            def step_first(b, par):
                split_z(b - 1, 1 - par, 0)
                split_x(b, NG - 1)
                split_x(b + 1, 0)
                start_softmax(b - 1, 1 - par)
                finish_first(b - 1, 1 - par)
                find_hits(b - 1)
                split_x(b + 1, 1)
                mix_weights(b, b)
                split_x(b + 1, 2)

            step_first(1, 1)
            step_first(2, 0)
            with dve.Fori(0, B // 2 - 2) as pair:
                b = 2 * pair + 3
                step_first(b, 1)
                step_first(b + 1, 0)

            split_z(B - 2, 0, 0)
            split_x(B - 1, NG - 1)
            for g in range(NG - 1):
                split_x(B, g)
                for t in range(KT + g * GROUP, KT + (g + 1) * GROUP):
                    split_w(t)
                if g == 0:
                    start_softmax(B - 2, 0)
                    finish_first(B - 2, 0)
                    find_hits(B - 2)
                if g == 1:
                    mix_weights(B - 1, B - 1)

            split_z(B - 1, 1, 0)
            split_x(B, NG - 1)
            for t in range(2 * KT - GROUP, 2 * KT):
                split_w(t)
            split_x(B + 1, 0)
            start_softmax(B - 1, 1)
            finish_first(B - 1, 1)
            find_hits(B - 1)
            dve.wait_ge(hits_merged, B)
            nc.vector.tensor_copy(any_hit[:, 1, :], any_hit[:, 0, :]).then_inc(any_hit_doubled, 1)
            split_x(B + 1, 1)
            mix_weights(0, B)
            split_x(B + 1, 2)
            dve.wait_ge(counts_made, 1)
            nc.vector.tensor_scalar(sel_bc[:, :], z_ps[0][:, 2, 0:P], 0.5, None, ALU.is_gt).then_inc(sel_ready, 1)
            copy_rowsum(1)
            dve.wait_ge(rowsum_ready, 2)
            dve.wait_ge(bias_in, 32)

            def copy_mask(half):
                for c in range(2):
                    at = half * HALF + c * BANK
                    dve.wait_ge(mask_made, 2 * (1 - half) + c + 1)
                    nc.vector.tensor_copy(row_mask[:, at:at + BANK], z_ps[c][:, 2, :]).then_inc(mask_ready, 1)

            def step_second(b, par):
                s = b + B
                split_z(s - 1, 1 - par, 1)
                split_x(s, NG - 1)
                if not isinstance(b, int) or b >= 2:
                    dve.wait_ge(out_ready, b - 1)
                make_offset(temp[:, :], b - 1, s - 1)
                sum_experts(b, s, w_sum)
                split_x(s + 1, 0)
                if isinstance(b, int) and b == 1:
                    for half in (1, 0):
                        copy_mask(half)
                    dve.wait_ge(mask_ready, 4)
                finish_second(b - 1, s - 1, 1 - par)
                split_agg(s)
                split_x(s + 1, 1)
                split_x(s + 1, 2)

            step_second(1, 1)
            step_second(2, 0)
            with dve.Fori(0, B // 2 - 2) as pair:
                b = 2 * pair + 3
                step_second(b, 1)
                step_second(b + 1, 0)

            split_z(2 * B - 2, 0, 1)
            split_x(2 * B - 1, NG - 1)
            dve.wait_ge(out_ready, B - 2)
            make_offset(temp[:, :], B - 2, 2 * B - 2)
            sum_experts(B - 1, 2 * B - 1, w_sum)
            rows = rest(1)
            spare = x_raw[:, :, :].rearrange("p k i -> p (k i)")
            scale, base = spare[:, 0:HALF], spare[:, HALF:H]
            sel = query_sel[:, B - 1:B]
            dve.wait_ge(rest_in[1], 2 * turn(B - 1, 1))
            nc.vector.scalar_tensor_tensor(out=first_half[:, 1, :], in0=first_half[:, 1, :], scalar=sel,
                                           in1=row_mask[:, 0:HALF], op0=ALU.mult,
                                           op1=ALU.mult).then_inc(tail_half_masked, 1)
            dve.wait_ge(tail_half_masked, 1)
            nc.vector.tensor_tensor(rows[:, 0:HALF], rows[:, 0:HALF], first_half[:, 1, :],
                                    ALU.add).then_inc(tail_half_ready, 1)
            finish_second(B - 2, 2 * B - 2, 0)
            split_agg(2 * B - 1)

            def tail_split(c):
                a, e = TAIL[c]
                dve.wait_ge(tail_hi, c + 1)
                nc.vector.tensor_tensor(z_lo[:, a:e], z_ps[1][:, c, 0:e - a], z_hi[:, a:e].bitcast(F32),
                                        ALU.subtract).then_inc(tail_lo, 1)

            def tail_finish(c):
                a, e = TAIL[c]
                dve.wait_ge(tail_dense, c + 1)
                nc.vector.tensor_tensor(temp[:, a:e], z_ps[0][:, c, 0:e - a], scale[:, a:e],
                                        ALU.mult).then_inc(tail_scaled, 1)
                dve.wait_ge(tail_scaled, c + 1)
                nc.vector.tensor_tensor(rows[:, HALF + a:HALF + e], rows[:, HALF + a:HALF + e], temp[:, a:e],
                                        ALU.add).then_inc(tail_ready, 1)

            tail_split(0)
            dve.wait_ge(x_lo_ready, NG * 2 * B)
            nc.vector.tensor_scalar(scale, row_mask[:, HALF:H], sel, None, ALU.mult).then_inc(tail_scale, 1)
            tail_split(1)
            make_offset(base, B - 1, 2 * B - 1)
            dve.wait_ge(tail_scale, 1)
            nc.vector.tensor_tensor(base, base, scale, ALU.mult).then_inc(tail_masked_offset, 1)
            dve.wait_ge(tail_masked_offset, 1)
            nc.vector.tensor_tensor(rows[:, HALF:H], rows[:, HALF:H], base, ALU.add).then_inc(tail_base, 1)
            dve.wait_ge(out_ready, B - 1)
            dve.wait_ge(tail_base, 1)
            tail_finish(0)
            tail_split(2)
            tail_finish(1)
            tail_finish(2)

        @block.tensor
        def _(pe):
            def group(s, par, phase, g, w_tile=None, small=None):
                pe.wait_ge(x_lo_ready, NG * s + g + 1)
                if g == 0 and (not isinstance(s, int) or s >= 2):
                    pe.wait_ge(z_lo_ready, s - 1)
                    if phase == 0:
                        pe.wait_ge(scores_ready, s - 1)
                for k in range(g * GROUP, (g + 1) * GROUP):
                    if w_tile is not None:
                        pe.wait_ge(w_lo_ready, w_tile + k + 1)
                    for xt, wt in ((x_hi, w_hi), (x_hi, w_lo), (x_lo, w_hi)):
                        for c, (a, e) in enumerate(CHUNKS[phase]):
                            last = nc.tensor.matmul(z_ps[par][:, c, 0:e - a], xt[:, k, :], wt[:, k, a:e],
                                                    start=(k == 0 and xt is x_hi and wt is w_hi),
                                                    stop=(k == KT - 1 and xt is x_lo))
                    if small is not None and k == (g + 1) * GROUP - 1:
                        last.then_inc(tiles_used, 1)
                        small(k)
                    elif k == (g + 1) * GROUP - 1:
                        last.then_inc(tiles_used, 1)
                    elif small is not None:
                        small(k)

            def mixed(dst, a, e):
                for n, (wt, zt) in enumerate(((agg_hi, z_hi), (agg_hi, z_lo), (agg_lo, z_hi))):
                    last = nc.tensor.matmul(dst, wt[:, :], zt[:, a:e], start=(n == 0), stop=(n == 2))
                return last

            def mix(s, par, phase):
                pe.wait_ge(agg_ready, s + 1)
                pe.wait_ge(z_lo_ready, s + 1)
                if phase == 0:
                    mixed(z_ps[par][:, 2, DOTS_AT:DOTS_AT + NC], HALF, WIDE).then_inc(dots_ready, 1)
                for c in range(2):
                    last = mixed(d_ps[:, c, :], c * BANK, (c + 1) * BANK)
                last.then_inc(dense_ready, 1)

            row_sums = [(d_ps[:, 0, :], 0, BANK), (d_ps[:, 1, :], BANK, HALF), (z_ps[1][:, 2, 0:NC], HALF, WIDE)]

            def sum_tile(t):
                for wt in (w_hi, w_lo):
                    for dst, a, e in row_sums:
                        nc.tensor.matmul(dst, ones_r[:, :], wt[:, t, a:e], start=(t == 1 and wt is w_hi), stop=False)

            def sum_rows(phase):
                pe.wait_ge(w_summed, len(SUMMED) + KT * phase)
                for dst, a, e in row_sums[0:3 - phase]:
                    last = nc.tensor.matmul(dst, ones, w_sum[:, a:e], start=(phase == 1), stop=True)
                last.then_inc(rowsum_made, 1)

            def small(k):
                if k == 0:
                    pe.wait_ge(small_done, 16)
                    nc.tensor.matmul(h1_ps, w0_sb, cond_sb, start=True, stop=True).then_inc(h1_made, 1)
                if k == 3:
                    pe.wait_ge(h1_ready, 1)
                    nc.tensor.matmul(h2_ps, w1_sb, h1, start=True, stop=True).then_inc(h2_made, 1)
                if k == 6:
                    pe.wait_ge(h2_ready, 1)
                    nc.tensor.matmul(logit_ps, h2, w2_sb, start=True, stop=False)
                    nc.tensor.matmul(logit_ps, ones[0:1, 0:B], b2_sb, start=False, stop=True).then_inc(logits_made, 1)
                if k == 12:
                    pe.wait_ge(att_diag_ready, 1)
                    nc.tensor.matmul(att_ps, ones[0:B, :], att_diag, start=True, stop=True).then_inc(att_spread, 1)
                if k not in SUMMED:
                    if k == 1:
                        pe.wait_ge(ones_ready, 1)
                    sum_tile(k)

            for g in range(NG):
                group(0, 0, 0, g, w_tile=0, small=small)
            sum_rows(0)
            pe.wait_ge(att_bc_ready, 1)

            def step_first(b, par):
                group(b, par, 0, 0)
                pe.wait_ge(rowsum_ready, 1)
                if not isinstance(b, int) or b >= 2:
                    pe.wait_ge(half_ready, b - 1)
                mix(b - 1, 1 - par, 0)
                for g in range(1, NG):
                    group(b, par, 0, g)

            pe.wait_ge(cluster_sum_ready, 1)
            step_first(1, 1)
            step_first(2, 0)
            with pe.Fori(0, B // 2 - 2) as pair:
                b = 2 * pair + 3
                step_first(b, 1)
                step_first(b + 1, 0)
            step_first(B - 1, 1)

            group(B, 0, 1, 0, w_tile=KT)
            group(B, 0, 1, 1, w_tile=KT)
            pe.wait_ge(half_ready, B - 1)
            mix(B - 1, 1, 0)
            group(B, 0, 1, 2, w_tile=KT)
            group(B, 0, 1, 3, w_tile=KT)
            pe.wait_ge(any_hit_doubled, 1)
            nc.tensor.matmul(z_ps[0][:, 2, 0:P], any_hit[:, :, :].rearrange("p a n -> p (a n)"), ones,
                             start=True, stop=True).then_inc(counts_made, 1)
            pe.wait_ge(half_ready, B)
            sum_rows(1)

            def make_mask(half):
                rows = slice(half * NC, (half + 1) * NC)
                for c in range(2):
                    if half == 0:
                        pe.wait_ge(mask_ready, c + 1)
                    nc.tensor.matmul(z_ps[c][:, 2, :], sel_bc[rows, :], onehot[rows, c * BANK:(c + 1) * BANK],
                                     start=True, stop=True).then_inc(mask_made, 1)

            def step_second(b, par):
                first = isinstance(b, int) and b == 1
                group(b + B, par, 1, 0)
                if first:
                    pe.wait_ge(sel_ready, 1)
                    make_mask(1)
                pe.wait_ge(rowsum_ready, 2)
                if not first:
                    pe.wait_ge(dense_drained, b - 1)
                mix(b + (B - 1), 1 - par, 1)
                for g in range(1, NG):
                    group(b + B, par, 1, g)
                    if first and g == 1:
                        make_mask(0)

            step_second(1, 1)
            step_second(2, 0)
            with pe.Fori(0, B // 2 - 2) as pair:
                b = 2 * pair + 3
                step_second(b, 1)
                step_second(b + 1, 0)

            def tail_mix(c):
                a, e = TAIL[c]
                pe.wait_ge(tail_lo, c + 1)
                pe.wait_ge(agg_ready, 2 * B)
                pe.wait_ge(z_lo_ready, 2 * B - 1)
                mixed(z_ps[0][:, c, 0:e - a], a, e).then_inc(tail_dense, 1)

            for c, (a, e) in enumerate(TAIL):
                if c == 0:
                    pe.wait_ge(z_lo_ready, 2 * B - 2)
                    pe.wait_ge(mask_ready, 4)
                for k in range(KT):
                    if c == 0 and k % GROUP == 0:
                        pe.wait_ge(x_lo_ready, NG * (2 * B - 1) + k // GROUP + 1)
                    for xt, wt in ((x_hi, w_hi), (x_hi, w_lo), (x_lo, w_hi)):
                        last = nc.tensor.matmul(z_ps[1][:, c, 0:e - a], xt[:, k, :], wt[:, k, a:e],
                                                start=(k == 0 and xt is x_hi and wt is w_hi),
                                                stop=(k == KT - 1 and xt is x_lo))
                    if c == 0 and k == KT // 2:
                        pe.wait_ge(dense_drained, B - 2)
                        mix(2 * B - 2, 0, 1)
                last.then_inc(tail_z, 1)
                if c >= 1:
                    tail_mix(c - 1)
            tail_mix(len(TAIL) - 1)


def small_columns(P, B, K):
    return [("W0", P), ("W1", P), ("cond_T", B), ("W2", K), ("bias_k_T", K), ("b2", K), ("b0", 1), ("b1", 1)]


def kernel(**inputs):
    import concourse.bacc as bacc
    from concourse.bass_utils import run_bass_kernel_spmd

    x = np.ascontiguousarray(inputs["x"])
    B, T, H = x.shape
    kt, half = H // P, H // 2
    weight_T = np.asarray(inputs["L0_ffn_weight"]).T.reshape(kt, P, H)
    centroids_T = np.asarray(inputs["L0_ffn_centroids"]).T.reshape(kt, P, -1)
    K = inputs["L0_cond_W2"].shape[1]
    parts = {
        "W0": inputs["L0_cond_W0"],
        "W1": inputs["L0_cond_W1"],
        "W2": inputs["L0_cond_W2"],
        "cond_T": np.asarray(inputs["cond_128"]).T,
        "bias_k_T": np.asarray(inputs["L0_cond_bias_k"]).T,
        "b0": np.asarray(inputs["L0_cond_b0"])[:, None],
        "b1": np.asarray(inputs["L0_cond_b1"])[:, None],
        "b2": np.asarray(inputs["L0_cond_b2"])[None, :],
    }
    columns = small_columns(P, B, K)
    small = np.zeros((P, sum(width for _, width in columns)), x.dtype)
    at = 0
    for name, width in columns:
        part = np.asarray(parts[name])
        small[:part.shape[0], at:at + width] = part
        at += width
    arrays = {
        "x": x,
        "xT": x.transpose(0, 2, 1).reshape(B, kt, P, T).transpose(0, 2, 1, 3),
        "w_first": np.concatenate([weight_T[:, :, :half], centroids_T], axis=2),
        "w_second": weight_T[:, :, half:],
        "small": small,
        "wk_T": np.asarray(inputs["L0_cond_weight"])[..., 0].transpose(2, 1, 0),
        "ffn_bias": inputs["L0_ffn_bias"],
        "assignments": inputs["L0_ffn_assignments"],
    }
    nc = bacc.Bacc("TRN2", target_bir_lowering=False, num_devices=1, dynamic_dma_scratch_size=1024)
    feed, args = {}, []
    for name, a in arrays.items():
        feed[f"in_{name}"] = np.ascontiguousarray(a)
        a = feed[f"in_{name}"]
        args.append(nc.dram_tensor(f"in_{name}", a.shape, mybir.dt.from_np(a.dtype), kind="ExternalInput").ap())
    args.append(nc.dram_tensor("out", x.shape, F32, kind="ExternalOutput").ap())
    adaln_ffn_kernel(nc, *args)
    r = run_bass_kernel_spmd(nc, [feed], core_ids=[0])
    return r.results[0]["out"]
```
